# Optimizing a Trainium2 kernel written in Bass

```python
import numpy as np
import jax
import jax.numpy as jnp

def _softmax(x, axis=-1):
    return jax.nn.softmax(x, axis=axis)
def _gelu(x):
    return jax.nn.gelu(x, approximate=True)
def _silu(x):
    return jax.nn.silu(x)
def _sigmoid(x):
    return jax.nn.sigmoid(x)
def _layernorm(x, axis=-1, eps=1e-5):
    m = jnp.mean(x, axis=axis, keepdims=True)
    v = jnp.var(x, axis=axis, keepdims=True)
    return (x - m) / jnp.sqrt(v + eps)
def _scatter_add(tgt, idx, src, axis=0):
    return tgt.at[idx].add(src)
def _segment_sum(src, seg, n):
    return jax.ops.segment_sum(src, seg, n)

kernel_name = 'mk_conv_seq_d4_conv_nchw16_583793'

def setup_inputs(seed: int = 0):
    np.random.seed(seed)
    _w = jnp.asarray
    def _rec_inputs():
        import jax
        import jax.numpy as jnp
        _gk = jax.random.key(seed)
        x = -7.109e-05 + 0.9999 * jax.random.normal(jax.random.fold_in(_gk, 1), (1, 16, 2048, 2048), jnp.float32)
        return x
    x = _rec_inputs()
    def _L0_conv_setup():
        import jax, jax.numpy as jnp
        import numpy as np
        B, N, T, S = (1, 16, 2048, 2048)
        G, I = (1, 2)
        M = N // G
        key = jax.random.key(seed)
        ks = jax.random.split(key, 8)
        return {'inputs': jax.random.normal(ks[0], (B, N, T, S), dtype=jnp.float32), 'qw1': jax.random.normal(ks[1], (B, T, G, I, M), dtype=jnp.float32) * 0.05, 'qw2': jax.random.normal(ks[2], (B, T, G, I, M), dtype=jnp.float32) * 0.05, 'kw1': jax.random.normal(ks[3], (B, S, G, I, M), dtype=jnp.float32) * 0.05, 'kw2': jax.random.normal(ks[4], (B, S, G, I, M), dtype=jnp.float32) * 0.05, 'qdd': jax.random.normal(ks[5], (B, T, G, M), dtype=jnp.float32) * 0.05, 'kdd': jax.random.normal(ks[6], (B, S, G, M), dtype=jnp.float32) * 0.05, 'w': jax.random.normal(ks[7], (G, M, M), dtype=jnp.float32) * 0.02}
    _L0_conv_all = _L0_conv_setup()
    _L0_conv_in = {k: v for k, v in _L0_conv_all.items() if k in ('qw1', 'qw2', 'kw1', 'kw2', 'qdd', 'kdd', 'w', )}
    del _L0_conv_all

    def _L1_conv_setup():
        import jax, jax.numpy as jnp
        import numpy as np
        B, N, T, S = (1, 16, 2048, 2048)
        G, I = (1, 2)
        M = N // G
        key = jax.random.key(seed)
        ks = jax.random.split(key, 8)
        return {'inputs': jax.random.normal(ks[0], (B, N, T, S), dtype=jnp.float32), 'qw1': jax.random.normal(ks[1], (B, T, G, I, M), dtype=jnp.float32) * 0.05, 'qw2': jax.random.normal(ks[2], (B, T, G, I, M), dtype=jnp.float32) * 0.05, 'kw1': jax.random.normal(ks[3], (B, S, G, I, M), dtype=jnp.float32) * 0.05, 'kw2': jax.random.normal(ks[4], (B, S, G, I, M), dtype=jnp.float32) * 0.05, 'qdd': jax.random.normal(ks[5], (B, T, G, M), dtype=jnp.float32) * 0.05, 'kdd': jax.random.normal(ks[6], (B, S, G, M), dtype=jnp.float32) * 0.05, 'w': jax.random.normal(ks[7], (G, M, M), dtype=jnp.float32) * 0.02}
    _L1_conv_all = _L1_conv_setup()
    _L1_conv_in = {k: v for k, v in _L1_conv_all.items() if k in ('qw1', 'qw2', 'kw1', 'kw2', 'qdd', 'kdd', 'w', )}
    del _L1_conv_all

    def _L2_conv_setup():
        import jax, jax.numpy as jnp
        import numpy as np
        B, H, T, S = (1, 16, 2048, 2048)
        G, I = (1, 2)
        M = H // G
        key = jax.random.key(seed)
        ks = jax.random.split(key, 8)
        scale = 0.02
        return {'inputs': jax.random.normal(ks[0], (B, H, T, S), dtype=jnp.float32), 'w': jax.random.normal(ks[1], (G, M, M), dtype=jnp.float32) * scale, 'qw1': jax.random.normal(ks[2], (B, T, G, I, M), dtype=jnp.float32) * scale, 'qw2': jax.random.normal(ks[3], (B, T, G, I, M), dtype=jnp.float32) * scale, 'kw1': jax.random.normal(ks[4], (B, S, G, I, M), dtype=jnp.float32) * scale, 'kw2': jax.random.normal(ks[5], (B, S, G, I, M), dtype=jnp.float32) * scale, 'qdd': jax.random.normal(ks[6], (B, T, G, M), dtype=jnp.float32) * scale, 'kdd': jax.random.normal(ks[7], (B, S, G, M), dtype=jnp.float32) * scale}
    _L2_conv_all = _L2_conv_setup()
    _L2_conv_in = {k: v for k, v in _L2_conv_all.items() if k in ('w', 'qw1', 'qw2', 'kw1', 'kw2', 'qdd', 'kdd', )}
    del _L2_conv_all

    def _L3_conv_setup():
        import jax, jax.numpy as jnp
        import numpy as np
        B, N, T, S = (1, 16, 2048, 2048)
        G, I = (1, 2)
        M = N // G
        key = jax.random.key(seed)
        ks = jax.random.split(key, 8)
        return {'inputs': jax.random.normal(ks[0], (B, N, T, S), dtype=jnp.float32), 'qw1': jax.random.normal(ks[1], (B, T, G, I, M), dtype=jnp.float32) * 0.05, 'qw2': jax.random.normal(ks[2], (B, T, G, I, M), dtype=jnp.float32) * 0.05, 'kw1': jax.random.normal(ks[3], (B, S, G, I, M), dtype=jnp.float32) * 0.05, 'kw2': jax.random.normal(ks[4], (B, S, G, I, M), dtype=jnp.float32) * 0.05, 'qdd': jax.random.normal(ks[5], (B, T, G, M), dtype=jnp.float32) * 0.05, 'kdd': jax.random.normal(ks[6], (B, S, G, M), dtype=jnp.float32) * 0.05, 'w': jax.random.normal(ks[7], (G, M, M), dtype=jnp.float32) * 0.02}
    _L3_conv_all = _L3_conv_setup()
    _L3_conv_in = {k: v for k, v in _L3_conv_all.items() if k in ('qw1', 'qw2', 'kw1', 'kw2', 'qdd', 'kdd', 'w', )}
    del _L3_conv_all

    return {
        "x": x,
        "L0_conv_qw1": _L0_conv_in["qw1"],
        "L0_conv_qw2": _L0_conv_in["qw2"],
        "L0_conv_kw1": _L0_conv_in["kw1"],
        "L0_conv_kw2": _L0_conv_in["kw2"],
        "L0_conv_qdd": _L0_conv_in["qdd"],
        "L0_conv_kdd": _L0_conv_in["kdd"],
        "L0_conv_w": _L0_conv_in["w"],
        "L1_conv_qw1": _L1_conv_in["qw1"],
        "L1_conv_qw2": _L1_conv_in["qw2"],
        "L1_conv_kw1": _L1_conv_in["kw1"],
        "L1_conv_kw2": _L1_conv_in["kw2"],
        "L1_conv_qdd": _L1_conv_in["qdd"],
        "L1_conv_kdd": _L1_conv_in["kdd"],
        "L1_conv_w": _L1_conv_in["w"],
        "L2_conv_w": _L2_conv_in["w"],
        "L2_conv_qw1": _L2_conv_in["qw1"],
        "L2_conv_qw2": _L2_conv_in["qw2"],
        "L2_conv_kw1": _L2_conv_in["kw1"],
        "L2_conv_kw2": _L2_conv_in["kw2"],
        "L2_conv_qdd": _L2_conv_in["qdd"],
        "L2_conv_kdd": _L2_conv_in["kdd"],
        "L3_conv_qw1": _L3_conv_in["qw1"],
        "L3_conv_qw2": _L3_conv_in["qw2"],
        "L3_conv_kw1": _L3_conv_in["kw1"],
        "L3_conv_kw2": _L3_conv_in["kw2"],
        "L3_conv_qdd": _L3_conv_in["qdd"],
        "L3_conv_kdd": _L3_conv_in["kdd"],
        "L3_conv_w": _L3_conv_in["w"],
    }

def reference(x, L0_conv_qw1, L0_conv_qw2, L0_conv_kw1, L0_conv_kw2, L0_conv_qdd, L0_conv_kdd, L0_conv_w, L1_conv_qw1, L1_conv_qw2, L1_conv_kw1, L1_conv_kw2, L1_conv_qdd, L1_conv_kdd, L1_conv_w, L2_conv_w, L2_conv_qw1, L2_conv_qw2, L2_conv_kw1, L2_conv_kw2, L2_conv_qdd, L2_conv_kdd, L3_conv_qw1, L3_conv_qw2, L3_conv_kw1, L3_conv_kw2, L3_conv_qdd, L3_conv_kdd, L3_conv_w):
    import jax
    import jax.numpy as jnp
    def _L0_conv_ref(inputs, qw1, qw2, kw1, kw2, qdd, kdd, w):
        import jax, jax.numpy as jnp
        import numpy as np
        B, N, T, S = (1, 16, 2048, 2048)
        G, I = (1, 2)
        M = N // G
        b, n, t, s = inputs.shape
        g, m = (w.shape[0], w.shape[1])
        x = inputs.reshape(b, g, m, t, s)
        wi = w + jnp.eye(m, dtype=w.dtype)
        ret = jnp.einsum('BGMTS,GMN->BGNTS', x, wi)
        hq = jnp.einsum('BGMTS,BTGIM->BGITS', x, qw1)
        ret = ret + jnp.einsum('BGITS,BTGIM->BGMTS', hq, qw2)
        hk = jnp.einsum('BGMTS,BSGIM->BGITS', x, kw1)
        ret = ret + jnp.einsum('BGITS,BSGIM->BGMTS', hk, kw2)
        ret = ret + jnp.einsum('BGMTS,BTGM->BGMTS', x, qdd)
        ret = ret + jnp.einsum('BGMTS,BSGM->BGMTS', x, kdd)
        return ret.reshape(b, n, t, s)

    def _L1_conv_ref(inputs, qw1, qw2, kw1, kw2, qdd, kdd, w):
        import jax, jax.numpy as jnp
        import numpy as np
        B, N, T, S = (1, 16, 2048, 2048)
        G, I = (1, 2)
        M = N // G
        b, n, t, s = inputs.shape
        g, m = (w.shape[0], w.shape[1])
        x = inputs.reshape(b, g, m, t, s)
        wi = w + jnp.eye(m, dtype=w.dtype)
        ret = jnp.einsum('BGMTS,GMN->BGNTS', x, wi)
        hq = jnp.einsum('BGMTS,BTGIM->BGITS', x, qw1)
        ret = ret + jnp.einsum('BGITS,BTGIM->BGMTS', hq, qw2)
        hk = jnp.einsum('BGMTS,BSGIM->BGITS', x, kw1)
        ret = ret + jnp.einsum('BGITS,BSGIM->BGMTS', hk, kw2)
        ret = ret + jnp.einsum('BGMTS,BTGM->BGMTS', x, qdd)
        ret = ret + jnp.einsum('BGMTS,BSGM->BGMTS', x, kdd)
        return ret.reshape(b, n, t, s)

    def _L2_conv_ref(inputs, w, qw1, qw2, kw1, kw2, qdd, kdd):
        import jax, jax.numpy as jnp
        import numpy as np
        B, H, T, S = (1, 16, 2048, 2048)
        G, I = (1, 2)
        M = H // G
        b, h, t, s = inputs.shape
        x = inputs.reshape(b, G, h // G, t, s)
        wI = w + jnp.eye(w.shape[-1], dtype=w.dtype)
        ret = jnp.einsum('BGMTS,GMN->BGNTS', x, wI)
        hq = jnp.einsum('BGMTS,BTGIM->BGITS', x, qw1)
        ret = ret + jnp.einsum('BGITS,BTGIM->BGMTS', hq, qw2)
        hk = jnp.einsum('BGMTS,BSGIM->BGITS', x, kw1)
        ret = ret + jnp.einsum('BGITS,BSGIM->BGMTS', hk, kw2)
        ret = ret + x * qdd.transpose(0, 2, 3, 1)[:, :, :, :, None]
        ret = ret + x * kdd.transpose(0, 2, 3, 1)[:, :, :, None, :]
        return ret.reshape(b, h, t, s)

    def _L3_conv_ref(inputs, qw1, qw2, kw1, kw2, qdd, kdd, w):
        import jax, jax.numpy as jnp
        import numpy as np
        B, N, T, S = (1, 16, 2048, 2048)
        G, I = (1, 2)
        M = N // G
        b, n, t, s = inputs.shape
        g, m = (w.shape[0], w.shape[1])
        x = inputs.reshape(b, g, m, t, s)
        wi = w + jnp.eye(m, dtype=w.dtype)
        ret = jnp.einsum('BGMTS,GMN->BGNTS', x, wi)
        hq = jnp.einsum('BGMTS,BTGIM->BGITS', x, qw1)
        ret = ret + jnp.einsum('BGITS,BTGIM->BGMTS', hq, qw2)
        hk = jnp.einsum('BGMTS,BSGIM->BGITS', x, kw1)
        ret = ret + jnp.einsum('BGITS,BSGIM->BGMTS', hk, kw2)
        ret = ret + jnp.einsum('BGMTS,BTGM->BGMTS', x, qdd)
        ret = ret + jnp.einsum('BGMTS,BSGM->BGMTS', x, kdd)
        return ret.reshape(b, n, t, s)

    def _gn(v, G=8, eps=1e-5):
        B_, C_, H_, W_ = v.shape
        g = v.reshape(B_, G, C_ // G, H_, W_)
        m = jnp.mean(g, axis=(2, 3, 4), keepdims=True)
        s = jnp.var(g, axis=(2, 3, 4), keepdims=True)
        return ((g - m) / jnp.sqrt(s + eps)).reshape(v.shape)

    def _ln_c(v, eps=1e-6):
        m = jnp.mean(v, axis=1, keepdims=True)
        s = jnp.var(v, axis=1, keepdims=True)
        return (v - m) / jnp.sqrt(s + eps)

    def _ln_t(v, eps=1e-5):
        m = jnp.mean(v, axis=-1, keepdims=True)
        s = jnp.var(v, axis=-1, keepdims=True)
        return (v - m) / jnp.sqrt(s + eps)

    def _to_tokens(v):
        B_, C_, H_, W_ = v.shape
        return v.reshape(B_, C_, H_ * W_).transpose(0, 2, 1)
    def _from_tokens(t, like):
        B_, C_, H_, W_ = like.shape
        return t.transpose(0, 2, 1).reshape(B_, C_, H_, W_)

    x = _L0_conv_ref(x, L0_conv_qw1, L0_conv_qw2, L0_conv_kw1, L0_conv_kw2, L0_conv_qdd, L0_conv_kdd, L0_conv_w)
    x = _L1_conv_ref(x, L1_conv_qw1, L1_conv_qw2, L1_conv_kw1, L1_conv_kw2, L1_conv_qdd, L1_conv_kdd, L1_conv_w)
    x = _L2_conv_ref(x, L2_conv_w, L2_conv_qw1, L2_conv_qw2, L2_conv_kw1, L2_conv_kw2, L2_conv_qdd, L2_conv_kdd)
    x = _L3_conv_ref(x, L3_conv_qw1, L3_conv_qw2, L3_conv_kw1, L3_conv_kw2, L3_conv_qdd, L3_conv_kdd, L3_conv_w)
    return x


_drawn_inputs = setup_inputs


def setup_inputs(seed=0):
    import zlib

    import numpy as np

    out = dict(_drawn_inputs(seed))
    spreads = {}
    factors = {'L0_conv_qw1': 4.154,
     'L0_conv_qw2': 4.139,
     'L0_conv_kw1': 4.121,
     'L0_conv_kw2': 4.127,
     'L1_conv_qw1': 4.221,
     'L1_conv_qw2': 4.202,
     'L1_conv_kw1': 4.192,
     'L1_conv_kw2': 4.196,
     'L2_conv_qw1': 8.0,
     'L2_conv_qw2': 8.0,
     'L2_conv_kw1': 8.0,
     'L2_conv_kw2': 8.0,
     'L2_conv_qdd': 2.857,
     'L2_conv_kdd': 2.848,
     'L3_conv_qw1': 4.156,
     'L3_conv_qw2': 4.133,
     'L3_conv_kw1': 4.131,
     'L3_conv_kw2': 4.134}
    for name, (base, spread) in spreads.items():
        noise = np.random.default_rng([zlib.crc32(name.encode()), seed]).standard_normal(out[name].shape)
        drawn = base * np.exp(spread * noise) if base else spread * noise
        out[name] = jnp.asarray(drawn.astype(out[name].dtype))
    for name, factor in factors.items():
        out[name] = (out[name] * factor).astype(out[name].dtype)
    return out
```

```python
from contextlib import ExitStack

import concourse.bass as bass
from concourse import mybir

F32 = mybir.dt.float32
ALU = mybir.AluOpType
ACT = mybir.ActivationFunctionType

P = 128
C = 16
L = 4
RANK = 2
T = S = 2048
G8 = P // C
TC = 256
SC = P
TG = TC // G8
SG = SC // G8
CHUNKS = T // TC
PAIRS = S // SC // 2
FREE = C * TC
BANK = 512

UNITS = FREE // BANK
AG = BANK // P
BG = BANK // TC
MIX_BANKS = 4
BX_BANKS = 2
TR_BANKS = 2
STAGE = 4
DMA = 16

HALF = 16
A_UNITS = L * TG // HALF
RAW = HALF * C * RANK
COEF = HALF * (RANK + 1)
KS = 2 * RANK * C + C
POOL_C = 12
HK_OPS = RANK * (C - 1)
K2_OPS = RANK * C - POOL_C - 1
V_SLOTS = 4
B_STEPS, A_STEPS = 4, 5


class Step:

    def __init__(self, it, k, ch, pr, first=False, last=False, chunk_end=False):
        self.it, self.k, self.ch, self.pr = it, k, ch, pr
        self.first, self.last, self.chunk_end = first, last, chunk_end
        self.has_m, self.has_e = not (last and k == 4), not first
        self.m_slot, self.e_slot = k % 2, (k + 1) % 2
        self.m_layer = 0 if k in (0, 1, 4) else 2
        self.e_layer = 1 if k in (1, 2) else 3
        self.parity = k % 2
        self.tr_extra = UNITS * {0: 0, 1: 0, 2: 1, 3: 3, 4: 5}[k]

    def count(self, per_step, extra=0):
        return self.it * (4 * per_step) + (per_step * self.k + extra)

    def transposed(self, extra=0):
        return self.it * (6 * UNITS) + (self.tr_extra + extra)

    def pairs(self, per_pair, extra=0):
        return self.it * per_pair + extra


def build_program(nc, x_t, x_s, q_second, q_coef, k_second, k_coef, k_scalars, w, shapes, out):
    with ExitStack() as ctx:
        def sb(name, cols):
            return ctx.enter_context(nc.sbuf_tensor(name, [P, cols], F32))

        def sem(name):
            return ctx.enter_context(nc.semaphore(name))

        by_t = [sb(f"by_t{x}", FREE) for x in "ab"]
        by_s = [sb(f"by_s{x}", FREE) for x in "ab"]
        pixels = [sb(f"pixels{x}", FREE) for x in "ab"]
        stage = sb("stage", STAGE * BANK)
        a_table = [sb(f"a_table{l}", TG * P) for l in range(L)]
        b_table = [sb(f"b_table{j}", SG * P) for j in range(2)]
        b_second = [sb(f"b_second{j}", RAW) for j in range(2)]
        b_coef = [sb(f"b_coef{j}", COEF) for j in range(2)]
        a_second = [sb(f"a_second{j}", RAW) for j in range(2)]
        a_coef = [sb(f"a_coef{j}", COEF) for j in range(2)]
        rank_terms = sb("rank_terms", RAW)
        diag_terms = sb("diag_terms", HALF * C)
        compact = sb("compact", HALF * C)
        hk = sb("hk", 2 * RANK * TC)
        v = sb("v", V_SLOTS * TC)
        kscal = [sb(f"kscal{j}", KS) for j in range(2)]
        w_eye = sb("w_eye", L * C)
        consts = sb("consts", P + 2 * G8 + 2 * C)
        ident = consts[:, 0:P]
        same_t = consts[:, P:P + G8]
        same_s = consts[:, P + G8:P + 2 * G8]
        eye_t = consts[:, P + 2 * G8:P + 2 * G8 + C]
        eye_s = consts[:, P + 2 * G8 + C:]

        mix_psum = [ctx.enter_context(nc.psum_tensor(f"mix_psum{i}", [P, BANK], F32)) for i in range(MIX_BANKS)]
        bx_psum = [ctx.enter_context(nc.psum_tensor(f"bx_psum{i}", [P, BANK], F32)) for i in range(BX_BANKS)]
        tr_psum = [ctx.enter_context(nc.psum_tensor(f"tr_psum{i}", [P, BANK], F32)) for i in range(TR_BANKS)]

        consts_in = sem("consts_in")
        by_t_in = [sem(f"by_t_in_{x}") for x in "ab"]
        by_s_in = [sem(f"by_s_in_{x}") for x in "ab"]
        by_s_moved = [sem(f"by_s_moved_{x}") for x in "ab"]
        bx_moved = [sem(f"bx_moved{j}") for j in range(STAGE)]
        stored = [sem(f"stored_{x}") for x in "ab"]
        b_raw_in = [sem(f"b_raw_in{j}") for j in range(2)]
        a_raw_in = [sem(f"a_raw_in{j}") for j in range(2)]
        kscal_in = [sem(f"kscal_in{j}") for j in range(2)]
        transposed = sem("transposed")
        bx_ready = sem("bx_ready")
        mixed = sem("mixed")
        by_t_copied = sem("by_t_copied")
        bx_staged = sem("bx_staged")
        hk_begun = sem("hk_begun")
        scaled = sem("scaled")
        v_ready = sem("v_ready")
        hk_added = sem("hk_added")
        added = sem("added")
        k2_added = sem("k2_added")
        v_added = sem("v_added")
        e_complete = sem("e_complete")
        w_eye_ready = sem("w_eye_ready")
        a_table_step = sem("a_table_step")
        b_table_step = sem("b_table_step")
        b_built = sem("b_built")
        a_built = sem("a_built")

        block = ctx.enter_context(nc.Block())

        def channel(slot, c):
            return pixels[slot][:, c * TC:(c + 1) * TC]

        def pixel_unit(slot, u):
            return pixels[slot][:, :].rearrange("s (q g) -> s q g", g=TG)[:, :, u * AG:(u + 1) * AG]

        def hk_of(step, i):
            j = step.parity * RANK + i
            return hk[:, j * TC:(j + 1) * TC]

        def k1(step, i, c):
            j = i * C + c
            return kscal[step.parity][:, j:j + 1]

        def k2(step, i, c):
            j = (RANK + i) * C + c
            return kscal[step.parity][:, j:j + 1]

        def kdd(step, c):
            return kscal[step.parity][:, 2 * RANK * C + c:2 * RANK * C + c + 1]

        def for_all_steps(eng, body, prologue):
            prologue()

            def pair(ch, pr, chunk_end=False, last=False):
                it = eng.snap(ch * PAIRS + pr) if not (isinstance(ch, int) and isinstance(pr, int)) else ch * PAIRS + pr
                for k in (1, 2, 3, 4):
                    body(Step(it, k, ch, pr, last=last, chunk_end=chunk_end))

            with eng.Fori(0, CHUNKS - 1) as ch:
                with eng.Fori(0, PAIRS - 1) as pr:
                    pair(ch, pr)
                pair(ch, PAIRS - 1, chunk_end=True)
            with eng.Fori(0, PAIRS - 1) as pr:
                pair(CHUNKS - 1, pr)
            pair(CHUNKS - 1, PAIRS - 1, last=True)

        step0 = Step(0, 0, 0, 0, first=True)

        @block.sync
        def _(sp):
            def load_by_t(slot, it):
                nc.sync.dma_start(by_t[slot][:, :], x_t[bass.ds(it * 2 + slot, 1)].rearrange("a p f -> (a p) f")
                                  ).then_inc(by_t_in[slot], DMA)

            def load_by_s(slot, it):
                nc.sync.dma_start(by_s[slot][:, :], x_s[bass.ds(it * 2 + slot, 1)].rearrange("a p f -> (a p) f")
                                  ).then_inc(by_s_in[slot], DMA)

            def load_b_raw(parity, half_layer, slot, pr):
                j = (pr * 2 + slot) * 2 + half_layer
                src = k_second[bass.ds(j, 1)].rearrange("a s f -> (a s) f").unsqueeze(1).to_broadcast([G8, C, RAW])
                nc.sync.dma_start(b_second[parity][:, :], src).then_inc(b_raw_in[parity], DMA)
                nc.sync.dma_start(b_coef[parity][:, :], k_coef[bass.ds(j, 1)].rearrange("a p f -> (a p) f")
                                  ).then_inc(b_raw_in[parity], DMA)

            def load_kscal(parity, half_layer, slot, pr):
                j = (pr * 2 + slot) * 2 + half_layer
                nc.sync.dma_start(kscal[parity][:, :], k_scalars[bass.ds(j, 1)].rearrange("a p f -> (a p) f")
                                  ).then_inc(kscal_in[parity], DMA)

            def move_bx(st):
                m = st.m_slot
                for u in range(UNITS):
                    sp.wait_ge(bx_staged, st.count(UNITS, u + 1))
                    for h in range(BG):
                        g = u * BG + h
                        src = stage[:, (u % STAGE) * BANK + h * TC:(u % STAGE) * BANK + (h + 1) * TC]
                        dst = pixels[m][g * G8:(g + 1) * G8, :].rearrange("s (c t) -> s c t", c=C)
                        nc.sync.dma_start(dst, src).then_inc(bx_moved[u % STAGE], DMA)

            def move_by_s(st):
                e = st.e_slot
                for g in range(SG):
                    src = pixels[e][g * G8:(g + 1) * G8, :].rearrange("s (c t) -> s c t", c=C)
                    nc.sync.dma_start(by_s[e][:, g * TC:(g + 1) * TC], src).then_inc(by_s_moved[e], DMA)

            def body(st):
                k = st.k
                nxt = 0 if st.chunk_end or st.last else st.pr + 1
                raw = {1: (1, 1, st.pr), 2: (0, 0, nxt), 3: (0, 1, nxt), 4: (1, 0, nxt)}[k]
                if k == 1 or (k <= 3 and not st.last):
                    sp.wait_ge(b_built, st.count(1, 1))
                    load_b_raw(st.parity, *raw)
                if not (st.last and k == 4):
                    src = {1: (0, 1, st.pr), 2: (1, 0, st.pr), 3: (1, 1, st.pr), 4: (0, 0, nxt)}[k]
                    sp.wait_ge(hk_added, st.count(HK_OPS, 1 - HK_OPS))
                    load_kscal(1 - st.parity, *src)
                if k == 3 and not st.last:
                    sp.wait_ge(bx_ready, st.count(UNITS))
                    load_by_s(0, st.it + 1)
                if k == 4 and not st.last:
                    sp.wait_ge(bx_ready, st.count(UNITS))
                    load_by_s(1, st.it + 1)
                    sp.wait_ge(stored[0], st.pairs(DMA, DMA))
                    load_by_t(0, st.it + 1)
                if st.has_m:
                    move_bx(st)
                sp.wait_ge(e_complete, st.count(1))
                e = st.e_slot
                if st.e_layer == 1:
                    move_by_s(st)
                else:
                    nc.sync.dma_start(out[bass.ds(st.it * 2 + e, 1)].rearrange("a p f -> (a p) f"),
                                      pixels[e][:, :]).then_inc(stored[e], DMA)
                if k == 4 and not st.last:
                    load_by_t(1, st.it + 1)
                if k == 4:
                    sp.wait_ge(stored[1], st.pairs(DMA, DMA))
                    if st.last:
                        sp.wait_ge(stored[0], st.pairs(DMA, DMA))
                    else:
                        load_b_raw(st.parity, *raw)

            def prologue():
                nc.sync.dma_start(consts[:, :], shapes).then_inc(consts_in, DMA)
                nc.sync.dma_start(w_eye[:, :], w.unsqueeze(1).to_broadcast([C, G8, L * C])).then_inc(consts_in, DMA)
                load_b_raw(0, 0, 0, 0)
                load_b_raw(1, 0, 1, 0)
                load_kscal(1, 0, 0, 0)
                load_by_s(0, 0)
                load_by_t(0, 0)
                load_by_s(1, 0)
                load_by_t(1, 0)
                sp.wait_ge(b_built, 1)
                load_b_raw(0, 1, 0, 0)
                move_bx(step0)

            for_all_steps(sp, body, prologue)

        @block.tensor
        def _(pe):
            def transposes(st, slot, first_unit):
                for u in range(UNITS):
                    pe.wait_ge(by_t_copied, st.transposed(first_unit + u + 1))
                    for g in range(AG):
                        src = pixel_unit(slot, u)[:, :, g]
                        last = nc.tensor.matmul(tr_psum[u % TR_BANKS][:, g * P:(g + 1) * P], src, ident,
                                                is_transpose=True, start=True, stop=True)
                    last.then_inc(transposed, 1)

            def b_products(st):
                m = st.m_slot
                if st.m_layer == 0:
                    pe.wait_ge(by_s_in[m], (st.pairs(DMA, DMA * (2 if st.k == 4 else 1))))
                else:
                    pe.wait_ge(by_s_moved[m], st.pairs(SG * DMA, SG * DMA))
                pe.wait_ge(b_built, st.count(1, 1))
                for u in range(UNITS):
                    if not (st.first and u < BX_BANKS):
                        pe.wait_ge(bx_staged, st.count(UNITS, u + 1 - BX_BANKS))
                    for h in range(BG):
                        g = u * BG + h
                        last = nc.tensor.matmul(bx_psum[u % BX_BANKS][:, h * TC:(h + 1) * TC],
                                                b_table[st.parity][:, g * P:(g + 1) * P],
                                                by_s[m][:, g * TC:(g + 1) * TC], start=True, stop=True)
                    last.then_inc(bx_ready, 1)

            def a_products(st, slot, layer, unit0, tr_units):
                for u in range(UNITS):
                    if tr_units is not None:
                        pe.wait_ge(by_t_copied, st.transposed(tr_units + u + 1 + TR_BANKS))
                    if not (st.first and u < MIX_BANKS):
                        pe.wait_ge(added, st.count(2 * UNITS, unit0 + u + 1 - MIX_BANKS))
                    for g in range(AG):
                        j = u * AG + g
                        last = nc.tensor.matmul(mix_psum[u % MIX_BANKS][:, g * P:(g + 1) * P],
                                                by_t[slot][:, j * P:(j + 1) * P],
                                                a_table[layer][:, j * P:(j + 1) * P], start=True, stop=True)
                    last.then_inc(mixed, 1)

            def wait_a_table(st, layer, next_chunk=False):
                pe.wait_ge(a_built, st.ch * A_UNITS + (A_UNITS * next_chunk + 2 * (layer + 1)))

            def body(st):
                pe.wait_ge(added, st.count(2 * UNITS, -UNITS))
                transposes(st, st.e_slot, 0)
                if st.m_layer == 2:
                    pe.wait_ge(e_complete, st.count(1, -1))
                    transposes(st, st.m_slot, UNITS)
                if st.has_m:
                    b_products(st)
                wait_a_table(st, st.e_layer)
                a_products(st, st.e_slot, st.e_layer, -UNITS, 0)
                if st.has_m:
                    wait_a_table(st, st.m_layer, next_chunk=st.chunk_end and st.k == 4)
                    if st.m_layer == 0:
                        pe.wait_ge(by_t_in[st.m_slot], st.pairs(DMA, DMA * (2 if st.k == 4 else 1)))
                    a_products(st, st.m_slot, st.m_layer, 0, UNITS if st.m_layer == 2 else None)

            def prologue():
                pe.wait_ge(consts_in, 2 * DMA)
                b_products(step0)
                wait_a_table(step0, 0)
                pe.wait_ge(by_t_in[0], DMA)
                a_products(step0, 0, 0, 0, None)

            for_all_steps(pe, body, prologue)

        @block.scalar
        def _(act):
            def copy_transposes(st, slot, first_unit, after=None):
                for u in range(UNITS):
                    act.wait_ge(transposed, st.transposed(first_unit + u + 1))
                    nc.scalar.activation(by_t[slot][:, u * BANK:(u + 1) * BANK], tr_psum[u % TR_BANKS][:, :],
                                         ACT.Copy).then_inc(by_t_copied, 1)
                    if after:
                        after(u)

            def stage_bx(st, after=None):
                for u in range(UNITS):
                    act.wait_ge(bx_ready, st.count(UNITS, u + 1))
                    if not (st.first and u < STAGE):
                        act.wait_ge(bx_moved[u % STAGE], st.count(2 * BG * DMA, (u // STAGE) * BG * DMA))
                    nc.scalar.activation(stage[:, (u % STAGE) * BANK:(u % STAGE + 1) * BANK], bx_psum[u % BX_BANKS][:, :],
                                         ACT.Copy).then_inc(bx_staged, 1)
                    if after:
                        after(u)

            def scale_by_kdd(st, c):
                if c:
                    act.wait_ge(hk_added, st.count(HK_OPS, RANK * c - HK_OPS))
                ch = channel(st.e_slot, c)
                nc.scalar.activation(ch, ch, ACT.Copy, scale=kdd(st, c)).then_inc(scaled, 1)

            def body(st):
                act.wait_ge(kscal_in[st.parity], st.pairs(2 * DMA, DMA * {1: 1, 2: 1, 3: 2, 4: 2}[st.k]))
                act.wait_ge(added, st.count(2 * UNITS, -UNITS))
                for i in range(RANK):
                    nc.scalar.activation(hk_of(st, i), channel(st.e_slot, 0), ACT.Copy,
                                         scale=k1(st, i, 0)).then_inc(hk_begun, 1)
                copy_transposes(st, st.e_slot, 0)
                pending = list(range(C))

                def some(n):
                    def run(u):
                        for _ in range(n):
                            if pending:
                                scale_by_kdd(st, pending.pop(0))
                    return run

                if st.m_layer == 2:
                    copy_transposes(st, st.m_slot, UNITS, some(1))
                if st.has_m:
                    stage_bx(st, some(1 if st.m_layer == 2 else 2))
                some(C)(0)
                for c in range(POOL_C):
                    if c == 0:
                        act.wait_ge(hk_added, st.count(HK_OPS))
                    act.wait_ge(v_added, st.count(POOL_C, c + 1 - POOL_C))
                    j = c % V_SLOTS
                    nc.scalar.activation(v[:, j * TC:(j + 1) * TC], hk_of(st, 1), ACT.Copy,
                                         scale=k2(st, 1, c)).then_inc(v_ready, 1)

            def prologue():
                act.sem_inc(by_t_copied, TR_BANKS)
                stage_bx(step0)

            for_all_steps(act, body, prologue)

        @block.vector
        def _(dve):
            def add_mixed(st, slot, unit0, u):
                dve.wait_ge(mixed, st.count(2 * UNITS, unit0 + u + 1))
                dst = pixel_unit(slot, u)
                src = mix_psum[u % MIX_BANKS][:, :].rearrange("s (g q) -> s q g", g=AG)
                nc.vector.tensor_tensor(dst, src, dst, ALU.add).then_inc(added, 1)

            def bx_in_pixels(st):
                for j in range(STAGE):
                    dve.wait_ge(bx_moved[j], st.count(2 * BG * DMA, 2 * BG * DMA))

            def body(st):
                e = st.e_slot
                dve.wait_ge(kscal_in[st.parity], st.pairs(2 * DMA, DMA * {1: 1, 2: 1, 3: 2, 4: 2}[st.k]))
                dve.wait_ge(added, st.count(2 * UNITS, -UNITS))
                for c in range(1, C):
                    for i in range(RANK):
                        j = RANK * (c - 1) + i
                        if c == 1:
                            dve.wait_ge(hk_begun, st.count(RANK, i + 1 - RANK))
                        else:
                            dve.wait_ge(hk_added, st.count(HK_OPS, j - 1 - HK_OPS))
                        nc.vector.scalar_tensor_tensor(out=hk_of(st, i), in0=channel(e, c), scalar=k1(st, i, c),
                                                       in1=hk_of(st, i), op0=ALU.mult, op1=ALU.add
                                                       ).then_inc(hk_added, 1)
                dve.wait_ge(scaled, st.count(C))
                for u in range(UNITS):
                    add_mixed(st, e, -UNITS, u)
                terms = [(c, 0) for c in range(C)] + [(c, 1) for c in range(POOL_C, C)]
                units = list(range(UNITS)) if st.has_m else []
                dve.wait_ge(hk_added, st.count(HK_OPS))
                dve.wait_ge(added, st.count(2 * UNITS))
                for n, (c, i) in enumerate(terms[:-1]):
                    if i == 1:
                        dve.wait_ge(k2_added, st.count(K2_OPS, c + 1 - K2_OPS))
                    nc.vector.scalar_tensor_tensor(out=channel(e, c), in0=hk_of(st, i), scalar=k2(st, i, c),
                                                   in1=channel(e, c), op0=ALU.mult, op1=ALU.add
                                                   ).then_inc(k2_added, 1)
                    if n % 2 and n >= 3 and units:
                        if units[0] == 0:
                            bx_in_pixels(st)
                        add_mixed(st, st.m_slot, 0, units.pop(0))
                for u in units:
                    add_mixed(st, st.m_slot, 0, u)
                dve.wait_ge(k2_added, st.count(K2_OPS))
                dve.wait_ge(v_added, st.count(POOL_C, V_SLOTS))
                c, i = terms[-1]
                nc.vector.scalar_tensor_tensor(out=channel(e, c), in0=hk_of(st, i), scalar=k2(st, i, c),
                                               in1=channel(e, c), op0=ALU.mult, op1=ALU.add).then_inc(e_complete, 1)

            def prologue():
                bx_in_pixels(step0)
                for u in range(UNITS):
                    add_mixed(step0, 0, 0, u)

            for_all_steps(dve, body, prologue)

        @block.gpsimd
        def _(pool):
            def build_compact(second, coef, eye, w, step, before):
                grid = compact[:, :].rearrange("p (g c) -> p g c", c=C)
                diag = diag_terms[:, :].rearrange("p (g c) -> p g c", c=C)
                terms = rank_terms[:, :].rearrange("p (g i c) -> p g i c", i=RANK, c=C)
                nc.gpsimd.tensor_tensor(
                    rank_terms[:, :].rearrange("p (g c) -> p g c", c=C),
                    second[:, :].rearrange("p (g c) -> p g c", c=C),
                    coef[:, 0:HALF * RANK].unsqueeze(2).to_broadcast([P, HALF * RANK, C]), ALU.mult).then_inc(step, 1)
                pool.wait_ge(step, before + 1)
                nc.gpsimd.tensor_tensor(grid, terms[:, :, 0, :], terms[:, :, 1, :], ALU.add).then_inc(step, 1)
                nc.gpsimd.tensor_tensor(
                    diag, eye.unsqueeze(1).to_broadcast([P, HALF, C]),
                    coef[:, HALF * RANK:].unsqueeze(2).to_broadcast([P, HALF, C]), ALU.mult).then_inc(step, 1)
                pool.wait_ge(step, before + 3)
                nc.gpsimd.tensor_tensor(grid, grid, diag, ALU.add).then_inc(step, 1)
                pool.wait_ge(step, before + 4)
                if w is not None:
                    nc.gpsimd.tensor_tensor(grid, grid, w.unsqueeze(1).to_broadcast([P, HALF, C]),
                                            ALU.add).then_inc(step, 1)
                    pool.wait_ge(step, before + 5)
                return grid

            def build_b_table(parity, before):
                grid = build_compact(b_second[parity], b_coef[parity], eye_s, None, b_table_step, before)
                nc.gpsimd.tensor_tensor(
                    b_table[parity][:, :].rearrange("p (g s c) -> p g s c", s=G8, c=C),
                    grid.unsqueeze(2).to_broadcast([P, HALF, G8, C]),
                    same_s.unsqueeze(1).unsqueeze(3).to_broadcast([P, HALF, G8, C]), ALU.mult).then_inc(b_built, 1)

            def build_a_half(layer, half, before):
                build_compact(a_second[half], a_coef[half], eye_t, w_eye[:, layer * C:(layer + 1) * C],
                              a_table_step, before)
                nc.gpsimd.tensor_tensor(
                    a_table[layer][:, half * HALF * P:(half + 1) * HALF * P].rearrange("p (g t) -> p g t", t=G8),
                    compact[:, :].unsqueeze(2).to_broadcast([P, HALF * C, G8]),
                    same_t.unsqueeze(1).to_broadcast([P, HALF * C, G8]), ALU.mult).then_inc(a_built, 1)

            def build_b(st):
                par = 1 - st.parity
                loads = {0: 1, 1: 2, 2: 2, 3: 3, 4: 3}[st.k]
                pool.wait_ge(b_raw_in[par], st.pairs(2 * 2 * DMA, loads * 2 * DMA))
                pool.wait_ge(b_built, st.count(1, 1))
                halves = {1: 0, 2: 0, 3: 2, 4: 4}[st.k] if st.chunk_end else 0
                if st.first:
                    pool.wait_ge(a_built, 2)
                else:
                    pool.wait_ge(a_built, st.ch * A_UNITS + (A_UNITS + halves))
                    pool.wait_ge(bx_ready, st.count(UNITS))
                build_b_table(par, st.count(B_STEPS, B_STEPS))

            def load_a_raw(ch, layer, half):
                j = (ch * L + layer) * 2 + half
                src = q_second[bass.ds(j, 1)].to_broadcast([C, G8, RAW])
                nc.gpsimd.dma_start(a_second[half][:, :], src).then_inc(a_raw_in[half], DMA)
                nc.gpsimd.dma_start(a_coef[half][:, :], q_coef[bass.ds(j, 1)].rearrange("a p f -> (a p) f")
                                    ).then_inc(a_raw_in[half], DMA)

            def build_a(ch, layer, b_tables, free=None):
                for half in range(2):
                    if not (isinstance(ch, int) and ch == 0 and layer == 0):
                        pool.wait_ge(a_built, ch * A_UNITS + (2 * layer + half - 1))
                    load_a_raw(ch, layer, half)
                pool.wait_ge(b_built, b_tables)
                if free is not None:
                    pool.wait_ge(*free)
                for half in range(2):
                    pool.wait_ge(a_raw_in[half], ch * (L * 2 * DMA) + (layer + 1) * 2 * DMA)
                    if half or layer or not (isinstance(ch, int) and ch == 0):
                        pool.wait_ge(a_built, ch * A_UNITS + (2 * layer + half))
                    build_a_half(layer, half, ch * (A_UNITS * A_STEPS) + (2 * layer + half) * A_STEPS)

            def add_v(st):
                for c in range(POOL_C):
                    pool.wait_ge(v_ready, st.count(POOL_C, c + 1 - POOL_C))
                    pool.wait_ge(k2_added, st.count(K2_OPS, c + 1 - K2_OPS))
                    ch = channel(st.e_slot, c)
                    j = c % V_SLOTS
                    term = nc.gpsimd.tensor_tensor(ch, ch, v[:, j * TC:(j + 1) * TC], ALU.add)
                    term.then_inc(v_added, 1)

            def body(st):
                if not (st.last and st.k >= 3):
                    build_b(st)
                add_v(st)
                if st.chunk_end and st.k >= 2:
                    layer = st.k - 2
                    build_a(st.ch + 1, layer, st.count(1, 2), (mixed, st.count(2 * UNITS, -UNITS)))
                    if layer == 2:
                        build_a(st.ch + 1, 3, st.count(1, 2), (mixed, st.count(2 * UNITS)))

            def prologue():
                pool.sem_inc(v_added, V_SLOTS)
                pool.wait_ge(consts_in, 2 * DMA)
                w_rows = w_eye[:, :].rearrange("p (l c) -> p l c", c=C)
                nc.gpsimd.tensor_tensor(w_rows, w_rows, eye_t.unsqueeze(1).to_broadcast([P, L, C]),
                                        ALU.add).then_inc(w_eye_ready, 1)
                pool.wait_ge(b_raw_in[0], 2 * DMA)
                build_b_table(0, 0)
                pool.wait_ge(w_eye_ready, 1)
                build_a(0, 0, 1)
                build_b(step0)
                for layer in (1, 2, 3):
                    build_a(0, layer, 2)

            for_all_steps(pool, body, prologue)


MATMUL_LAYERS, ELEMENT_LAYERS = (0, 2), (1, 3)


def kernel(**inputs):
    import numpy as np
    import concourse.bacc as bacc
    from concourse.bass_utils import run_bass_kernel_spmd

    def per_layer(name):
        return [np.asarray(inputs[f"L{l}_conv_{name}"]) for l in range(L)]

    stiles, halves = S // SC, TG // HALF
    x = np.asarray(inputs["x"]).reshape(C, T, S)
    x_t = x.reshape(C, CHUNKS, G8, TG, stiles, SC).transpose(1, 4, 0, 2, 3, 5).reshape(-1, P, FREE)
    x_s = x.reshape(C, CHUNKS, TC, stiles, SG, G8).transpose(1, 3, 5, 0, 4, 2).reshape(-1, P, FREE)

    q1 = np.stack([a.reshape(CHUNKS, G8, halves, HALF, RANK, C) for a in per_layer("qw1")], 1)
    q2 = np.stack([a.reshape(CHUNKS, G8, halves, HALF, RANK, C) for a in per_layer("qw2")], 1)
    qd = np.stack([a.reshape(CHUNKS, G8, halves, HALF, C) for a in per_layer("qdd")], 1)
    q_second = q2.transpose(0, 1, 3, 2, 4, 5, 6).reshape(-1, G8, RAW)
    q_coef = np.concatenate([q1.transpose(0, 1, 3, 6, 2, 4, 5).reshape(-1, P, HALF * RANK),
                             qd.transpose(0, 1, 3, 5, 2, 4).reshape(-1, P, HALF)], 2)

    k1, k2, kd = per_layer("kw1"), per_layer("kw2"), per_layer("kdd")
    m1 = np.stack([k1[l].reshape(stiles, SG, G8, RANK, C) for l in MATMUL_LAYERS], 1)
    m2 = np.stack([k2[l].reshape(stiles, SG, G8, RANK, C) for l in MATMUL_LAYERS], 1)
    md = np.stack([kd[l].reshape(stiles, SG, G8, C) for l in MATMUL_LAYERS], 1)
    k_second = m2.transpose(0, 1, 3, 2, 4, 5).reshape(-1, G8, RAW)
    k_coef = np.concatenate([m1.transpose(0, 1, 3, 5, 2, 4).reshape(-1, P, SG * RANK),
                             md.transpose(0, 1, 3, 4, 2).reshape(-1, P, SG)], 2)
    k_scalars = np.stack([np.concatenate([k1[l].reshape(stiles, SC, RANK * C), k2[l].reshape(stiles, SC, RANK * C),
                                          kd[l].reshape(stiles, SC, C)], 2) for l in ELEMENT_LAYERS], 1)
    k_scalars = k_scalars.reshape(-1, P, KS)
    w = np.stack([a.reshape(C, C) for a in per_layer("w")], 1).reshape(C, L * C)

    p = np.arange(P)[:, None]
    shapes = np.concatenate([p == np.arange(P), p % G8 == np.arange(G8), p // C == np.arange(G8),
                             p // G8 == np.arange(C), p % C == np.arange(C)], 1).astype(np.float32)

    nc = bacc.Bacc("TRN2", target_bir_lowering=False, num_devices=1)
    arrays, args = {}, []
    for name, a in (("x_t", x_t), ("x_s", x_s), ("q_second", q_second), ("q_coef", q_coef), ("k_second", k_second),
                    ("k_coef", k_coef), ("k_scalars", k_scalars), ("w", w), ("shapes", shapes)):
        arrays[name] = np.ascontiguousarray(a)
        args.append(nc.dram_tensor(name, a.shape, F32, kind="ExternalInput").ap())
    args.append(nc.dram_tensor("out", (CHUNKS * stiles, P, FREE), F32, kind="ExternalOutput").ap())
    build_program(nc, *args)
    result = run_bass_kernel_spmd(nc, [arrays], core_ids=[0]).results[0]["out"]
    return result.reshape(CHUNKS, stiles, SC, C, TC).transpose(3, 0, 4, 1, 2).reshape(1, C, T, S)
```

```python
from contextlib import ExitStack

import concourse.bass as bass
from concourse import mybir

F32 = mybir.dt.float32
ALU = mybir.AluOpType
ACT = mybir.ActivationFunctionType

P = 128
C = 16
L = 4
RANK = 2
T = S = 2048
G8 = P // C
TC = 256
SC = P
TG = TC // G8
SG = SC // G8
CHUNKS = T // TC
PAIRS = S // SC // 2
FREE = C * TC
BANK = 512

UNITS = FREE // BANK
AG = BANK // P
BG = BANK // TC
MIX_BANKS = 4
BX_BANKS = 2
TR_BANKS = 2
TR_LAG = 3
STAGE = 4
DMA = 16

HALF = 16
A_UNITS = L * TG // HALF
RAW = HALF * C * RANK
COEF = HALF * (RANK + 1)
KS = 2 * RANK * C + C
POOL_C = 12
HK_OPS = RANK * C
K2_OPS = RANK * C - POOL_C - 1
EARLY_C = 8
OLD_AHEAD = 5
E_AFTER = 3
E_FROM = {0: UNITS, 2: 4}
SCALE_FIRST = 2
SCALE_PER_UNIT = {0: 2, 2: 1}
FILL_C = 2
ADD_FROM = {1: 4, 2: 8, 3: 8, 4: 10}
ADD_EVERY = 2
V_SLOTS = 4
END_BUILDS = {2: [0], 3: [1, 2], 4: [3, 4]}
START_BUILDS = {1: [5, 6], 2: [7]}
B_STEPS, A_STEPS = 4, 5


class Step:

    def __init__(self, it, k, ch, pr, first=False, last=False, chunk_end=False, chunk_start=False):
        self.it, self.k, self.ch, self.pr = it, k, ch, pr
        self.first, self.last, self.chunk_end, self.chunk_start = first, last, chunk_end, chunk_start
        self.has_m, self.has_e = not (last and k == 4), not first
        self.m_slot, self.e_slot = k % 2, (k + 1) % 2
        self.m_layer = 0 if k in (0, 1, 4) else 2
        self.e_layer = 1 if k in (1, 2) else 3
        self.parity = k % 2
        self.pool_late = chunk_end and k - 1 in END_BUILDS or chunk_start and (k == 1 or k - 1 in START_BUILDS)
        self.tr_extra = UNITS * {0: 0, 1: 1, 2: 2, 3: 4, 4: 6}[k]
        self.tr_new = UNITS if self.m_layer == 2 else 0

    def count(self, per_step, extra=0):
        return self.it * (4 * per_step) + (per_step * self.k + extra)

    def transposed(self, extra=0):
        return self.it * (6 * UNITS) + (self.tr_extra + extra)

    def pairs(self, per_pair, extra=0):
        return self.it * per_pair + extra


def build_program(nc, x_t, x_s, q_second, q_coef, k_second, k_coef, k_scalars, w, shapes, out):
    with ExitStack() as ctx:
        def sb(name, cols):
            return ctx.enter_context(nc.sbuf_tensor(name, [P, cols], F32))

        def sem(name):
            return ctx.enter_context(nc.semaphore(name))

        by_t = [sb(f"by_t{x}", FREE) for x in "ab"]
        by_s = [sb(f"by_s{x}", FREE) for x in "ab"]
        pixels = [sb(f"pixels{x}", FREE) for x in "ab"]
        stage = sb("stage", STAGE * BANK)
        a_table = [sb(f"a_table{l}", TG * P) for l in range(L)]
        b_table = [sb(f"b_table{j}", SG * P) for j in range(2)]
        b_second = [sb(f"b_second{j}", RAW) for j in range(2)]
        b_coef = [sb(f"b_coef{j}", COEF) for j in range(2)]
        a_second = [sb(f"a_second{j}", RAW) for j in range(2)]
        a_coef = [sb(f"a_coef{j}", COEF) for j in range(2)]
        rank_terms = sb("rank_terms", RAW)
        diag_terms = sb("diag_terms", HALF * C)
        compact = sb("compact", HALF * C)
        hk = sb("hk", 2 * RANK * TC)
        v = sb("v", V_SLOTS * TC)
        kscal = [sb(f"kscal{j}", KS) for j in range(2)]
        w_eye = sb("w_eye", L * C)
        consts = sb("consts", P + 2 * G8 + 2 * C)
        ident = consts[:, 0:P]
        same_t = consts[:, P:P + G8]
        same_s = consts[:, P + G8:P + 2 * G8]
        eye_t = consts[:, P + 2 * G8:P + 2 * G8 + C]
        eye_s = consts[:, P + 2 * G8 + C:]

        mix_psum = [ctx.enter_context(nc.psum_tensor(f"mix_psum{i}", [P, BANK], F32)) for i in range(MIX_BANKS)]
        bx_psum = [ctx.enter_context(nc.psum_tensor(f"bx_psum{i}", [P, BANK], F32)) for i in range(BX_BANKS)]
        tr_psum = [ctx.enter_context(nc.psum_tensor(f"tr_psum{i}", [P, BANK], F32)) for i in range(TR_BANKS)]

        consts_in = sem("consts_in")
        by_t_in = [sem(f"by_t_in_{x}") for x in "ab"]
        by_s_in = [sem(f"by_s_in_{x}") for x in "ab"]
        by_s_moved = [[sem(f"by_s_moved_{x}{u}") for u in range(UNITS)] for x in "ab"]
        bx_moved = [sem(f"bx_moved{j}") for j in range(STAGE)]
        stored = [sem(f"stored_{x}") for x in "ab"]
        b_raw_in = [sem(f"b_raw_in{j}") for j in range(2)]
        a_raw_in = [sem(f"a_raw_in{j}") for j in range(2)]
        kscal_in = [sem(f"kscal_in{j}") for j in range(2)]
        transposed = sem("transposed")
        bx_ready = sem("bx_ready")
        mixed = sem("mixed")
        by_t_copied = sem("by_t_copied")
        bx_staged = sem("bx_staged")
        scaled = sem("scaled")
        late_scaled = sem("late_scaled")
        v_ready = sem("v_ready")
        hk_added = sem("hk_added")
        added = sem("added")
        k2_added = sem("k2_added")
        v_added = sem("v_added")
        e_complete = sem("e_complete")
        w_eye_ready = sem("w_eye_ready")
        a_table_step = sem("a_table_step")
        b_table_step = sem("b_table_step")
        b_built = sem("b_built")
        a_built = sem("a_built")

        block = ctx.enter_context(nc.Block())

        def channel(slot, c):
            return pixels[slot][:, c * TC:(c + 1) * TC]

        def pixel_unit(slot, u):
            return pixels[slot][:, :].rearrange("s (q g) -> s q g", g=TG)[:, :, u * AG:(u + 1) * AG]

        def hk_of(step, i):
            j = step.parity * RANK + i
            return hk[:, j * TC:(j + 1) * TC]

        def k1(step, i, c):
            j = i * C + c
            return kscal[step.parity][:, j:j + 1]

        def k2(step, i, c):
            j = (RANK + i) * C + c
            return kscal[step.parity][:, j:j + 1]

        def kdd(step, c):
            return kscal[step.parity][:, 2 * RANK * C + c:2 * RANK * C + c + 1]

        def for_all_steps(eng, body, prologue):
            prologue()

            def pair(ch, pr, **flags):
                fixed = isinstance(ch, int) and isinstance(pr, int)
                it = ch * PAIRS + pr if fixed else eng.snap(ch * PAIRS + pr)
                for k in (1, 2, 3, 4):
                    body(Step(it, k, ch, pr, **flags))

            with eng.Fori(0, CHUNKS - 1) as ch:
                pair(ch, 0, chunk_start=True)
                with eng.Fori(1, PAIRS - 1) as pr:
                    pair(ch, pr)
                pair(ch, PAIRS - 1, chunk_end=True)
            pair(CHUNKS - 1, 0, chunk_start=True)
            with eng.Fori(1, PAIRS - 1) as pr:
                pair(CHUNKS - 1, pr)
            pair(CHUNKS - 1, PAIRS - 1, last=True)

        step0 = Step(0, 0, 0, 0, first=True)

        @block.sync
        def _(sp):
            def load_by_t(slot, it):
                nc.sync.dma_start(by_t[slot][:, :], x_t[bass.ds(it * 2 + slot, 1)].rearrange("a p f -> (a p) f")
                                  ).then_inc(by_t_in[slot], DMA)

            def load_by_s(slot, it):
                nc.sync.dma_start(by_s[slot][:, :], x_s[bass.ds(it * 2 + slot, 1)].rearrange("a p f -> (a p) f")
                                  ).then_inc(by_s_in[slot], DMA)

            def load_b_raw(parity, half_layer, slot, pr):
                j = (pr * 2 + slot) * 2 + half_layer
                src = k_second[bass.ds(j, 1)].rearrange("a s f -> (a s) f").unsqueeze(1).to_broadcast([G8, C, RAW])
                nc.sync.dma_start(b_second[parity][:, :], src).then_inc(b_raw_in[parity], DMA)
                nc.sync.dma_start(b_coef[parity][:, :], k_coef[bass.ds(j, 1)].rearrange("a p f -> (a p) f")
                                  ).then_inc(b_raw_in[parity], DMA)

            def load_kscal(parity, half_layer, slot, pr):
                j = (pr * 2 + slot) * 2 + half_layer
                nc.sync.dma_start(kscal[parity][:, :], k_scalars[bass.ds(j, 1)].rearrange("a p f -> (a p) f")
                                  ).then_inc(kscal_in[parity], DMA)

            def move_bx(st):
                m = st.m_slot
                for u in range(UNITS):
                    sp.wait_ge(bx_staged, st.count(UNITS, u + 1))
                    for h in range(BG):
                        g = u * BG + h
                        src = stage[:, (u % STAGE) * BANK + h * TC:(u % STAGE) * BANK + (h + 1) * TC]
                        dst = pixels[m][g * G8:(g + 1) * G8, :].rearrange("s (c t) -> s c t", c=C)
                        nc.sync.dma_start(dst, src).then_inc(bx_moved[u % STAGE], DMA)

            def move_by_s(st):
                e = st.e_slot
                for g in range(SG):
                    src = pixels[e][g * G8:(g + 1) * G8, :].rearrange("s (c t) -> s c t", c=C)
                    nc.sync.dma_start(by_s[e][:, g * TC:(g + 1) * TC], src).then_inc(by_s_moved[e][g // BG], DMA)

            def body(st):
                k = st.k
                nxt = 0 if st.chunk_end or st.last else st.pr + 1
                raw = {1: (1, 1, st.pr), 2: (0, 0, nxt), 3: (0, 1, nxt), 4: (1, 0, nxt)}[k]
                if k == 1:
                    move_bx(st)
                    sp.wait_ge(b_built, st.count(1, 1))
                    load_b_raw(st.parity, *raw)
                elif k <= 3:
                    sp.wait_ge(transposed, st.transposed(UNITS))
                    load_b_raw(st.parity, *raw)
                src = {1: (0, 1, st.pr), 2: (1, 0, st.pr), 3: (1, 1, st.pr), 4: (0, 0, nxt)}[k]
                if k == 4 and not st.last:
                    sp.wait_ge(stored[0], st.pairs(DMA, DMA))
                    load_kscal(1 - st.parity, *src)
                if st.has_m and k != 1:
                    move_bx(st)
                if k < 4:
                    sp.wait_ge(hk_added, st.count(HK_OPS, 1 - HK_OPS))
                    load_kscal(1 - st.parity, *src)
                if k >= 3 and not st.last:
                    e = st.e_slot
                    sp.wait_ge(bx_ready, st.count(UNITS))
                    load_by_s(e, st.it + 1)
                    sp.wait_ge(mixed, st.count(2 * UNITS))
                    load_by_t(e, st.it + 1)
                sp.wait_ge(e_complete, st.count(1))
                if st.e_layer == 1:
                    move_by_s(st)
                else:
                    nc.sync.dma_start(out[bass.ds(st.it * 2 + st.e_slot, 1)].rearrange("a p f -> (a p) f"),
                                      pixels[st.e_slot][:, :]).then_inc(stored[st.e_slot], DMA)
                if k == 4:
                    sp.wait_ge(stored[1], st.pairs(DMA, DMA))
                    if st.last:
                        sp.wait_ge(stored[0], st.pairs(DMA, DMA))
                        for j in range(2):
                            sp.wait_ge(b_raw_in[j], st.pairs(2 * 2 * DMA, 3 * 2 * DMA))
                    else:
                        load_b_raw(st.parity, *raw)

            def prologue():
                nc.sync.dma_start(consts[:, :], shapes).then_inc(consts_in, DMA)
                nc.sync.dma_start(w_eye[:, :], w.unsqueeze(1).to_broadcast([C, G8, L * C])).then_inc(consts_in, DMA)
                load_b_raw(0, 0, 0, 0)
                load_b_raw(1, 0, 1, 0)
                load_kscal(1, 0, 0, 0)
                load_by_s(0, 0)
                load_by_t(0, 0)
                sp.wait_ge(b_built, 1)
                load_b_raw(0, 1, 0, 0)
                move_bx(step0)
                load_by_s(1, 0)
                load_by_t(1, 0)

            for_all_steps(sp, body, prologue)

        @block.tensor
        def _(pe):
            def transpose_unit(st, slot, first_unit, u):
                pe.wait_ge(by_t_copied, st.transposed(first_unit + u + 1))
                for g in range(AG):
                    src = pixel_unit(slot, u)[:, :, g]
                    last = nc.tensor.matmul(tr_psum[u % TR_BANKS][:, g * P:(g + 1) * P], src, ident,
                                            is_transpose=True, start=True, stop=True)
                last.then_inc(transposed, 1)

            def b_products(st, before=None, between=None):
                m, m_layer_2 = st.m_slot, st.m_layer == 2
                if not m_layer_2:
                    pe.wait_ge(by_s_in[m], (st.pairs(DMA, DMA * (2 if st.k == 4 else 1))))
                pe.wait_ge(b_built, st.count(1, 1))
                for u in range(UNITS):
                    if before:
                        before(u)
                    if m_layer_2:
                        pe.wait_ge(by_s_moved[m][u], st.pairs(BG * DMA, BG * DMA))
                    if not (st.first and u < BX_BANKS):
                        pe.wait_ge(bx_staged, st.count(UNITS, u + 1 - BX_BANKS))
                    for h in range(BG):
                        g = u * BG + h
                        last = nc.tensor.matmul(bx_psum[u % BX_BANKS][:, h * TC:(h + 1) * TC],
                                                b_table[st.parity][:, g * P:(g + 1) * P],
                                                by_s[m][:, g * TC:(g + 1) * TC], start=True, stop=True)
                    last.then_inc(bx_ready, 1)
                    if between:
                        between(u)

            def a_product_unit(st, slot, layer, unit0, tr_unit, u):
                if tr_unit is not None:
                    pe.wait_ge(by_t_copied, st.transposed(tr_unit + u + 1 + TR_BANKS))
                if not (st.first and u < MIX_BANKS):
                    pe.wait_ge(added, st.count(2 * UNITS, unit0 + u + 1 - MIX_BANKS))
                for g in range(AG):
                    j = u * AG + g
                    last = nc.tensor.matmul(mix_psum[u % MIX_BANKS][:, g * P:(g + 1) * P],
                                            by_t[slot][:, j * P:(j + 1) * P],
                                            a_table[layer][:, j * P:(j + 1) * P], start=True, stop=True)
                last.then_inc(mixed, 1)

            def wait_a_table(st, layer, next_chunk=False):
                pe.wait_ge(a_built, st.ch * A_UNITS + (A_UNITS * next_chunk + 2 * (layer + 1)))

            def m_products(st, tr_unit):
                for u in range(UNITS + TR_LAG):
                    if u < UNITS:
                        a_product_unit(st, st.m_slot, st.m_layer, 0, tr_unit, u)
                    if u >= TR_LAG:
                        pe.wait_ge(added, st.count(2 * UNITS, u - TR_LAG + 1))
                        transpose_unit(st, st.m_slot, st.tr_new, u - TR_LAG)

            def body(st):
                def e_products(units):
                    for u in units:
                        a_product_unit(st, st.e_slot, st.e_layer, -UNITS, -UNITS, u)

                rest = list(range(UNITS))

                def some_e_products(count):
                    if count and len(rest) == UNITS:
                        wait_a_table(st, st.e_layer)
                    e_products([rest.pop(0) for _ in range(min(count, len(rest)))])

                if st.m_layer == 2:
                    pe.wait_ge(e_complete, st.count(1, -1))
                    for u in range(OLD_AHEAD):
                        transpose_unit(st, st.m_slot, 0, u)

                def transposes(u):
                    if u + OLD_AHEAD < UNITS:
                        transpose_unit(st, st.m_slot, 0, u + OLD_AHEAD)

                if st.has_m:
                    b_products(st, transposes if st.m_layer == 2 else None,
                               lambda u: some_e_products(MIX_BANKS if u == E_AFTER else
                                                         1 if u >= E_FROM[st.m_layer] else 0))
                some_e_products(UNITS)
                if st.has_m:
                    wait_a_table(st, st.m_layer, next_chunk=st.chunk_end and st.k == 4)
                    if st.m_layer == 0:
                        pe.wait_ge(by_t_in[st.m_slot], st.pairs(DMA, DMA * (2 if st.k == 4 else 1)))
                    m_products(st, 0 if st.m_layer == 2 else None)

            def prologue():
                pe.wait_ge(consts_in, 2 * DMA)
                b_products(step0)
                wait_a_table(step0, 0)
                pe.wait_ge(by_t_in[0], DMA)
                m_products(step0, None)

            for_all_steps(pe, body, prologue)

        @block.scalar
        def _(act):
            def copy_transpose(st, slot, first_unit, u):
                act.wait_ge(transposed, st.transposed(first_unit + u + 1))
                nc.scalar.activation(by_t[slot][:, u * BANK:(u + 1) * BANK], tr_psum[u % TR_BANKS][:, :],
                                     ACT.Copy).then_inc(by_t_copied, 1)

            def stage_bx(st, u):
                act.wait_ge(bx_ready, st.count(UNITS, u + 1))
                if not (st.first and u < STAGE):
                    act.wait_ge(bx_moved[u % STAGE], st.count(2 * BG * DMA, (u // STAGE) * BG * DMA))
                nc.scalar.activation(stage[:, (u % STAGE) * BANK:(u % STAGE + 1) * BANK], bx_psum[u % BX_BANKS][:, :],
                                     ACT.Copy).then_inc(bx_staged, 1)

            def scale_by_kdd(st, c):
                act.wait_ge(hk_added, st.count(HK_OPS, RANK * (c + 1) - HK_OPS))
                ch = channel(st.e_slot, c)
                nc.scalar.activation(ch, ch, ACT.Copy, scale=kdd(st, c)
                                     ).then_inc(scaled if c < EARLY_C else late_scaled, 1)

            def body(st):
                act.wait_ge(kscal_in[st.parity], st.pairs(2 * DMA, DMA * {1: 1, 2: 1, 3: 2, 4: 2}[st.k]))
                channels = list(range(C if st.pool_late else EARLY_C))

                def scale_some(count):
                    for _ in range(min(count, len(channels))):
                        scale_by_kdd(st, channels.pop(0))

                scale_some(2 * SCALE_FIRST if st.pool_late else SCALE_FIRST)
                if st.m_layer == 2:
                    for u in range(OLD_AHEAD):
                        copy_transpose(st, st.m_slot, 0, u)
                        scale_some(1)
                if st.has_m:
                    for u in range(UNITS):
                        if st.m_layer == 2 and u + OLD_AHEAD < UNITS:
                            copy_transpose(st, st.m_slot, 0, u + OLD_AHEAD)
                        stage_bx(st, u)
                        scale_some(2 if st.pool_late else SCALE_PER_UNIT[st.m_layer])
                scale_some(C)
                products = list(range(POOL_C))

                def multiply_some(count):
                    for _ in range(min(count, len(products))):
                        c = products.pop(0)
                        if c == 0:
                            act.wait_ge(hk_added, st.count(HK_OPS))
                        act.wait_ge(v_added, st.count(POOL_C, c + 1 - POOL_C))
                        j = c % V_SLOTS
                        nc.scalar.activation(v[:, j * TC:(j + 1) * TC], hk_of(st, 1), ACT.Copy,
                                             scale=k2(st, 1, c)).then_inc(v_ready, 1)

                multiply_some(POOL_C)
                if st.has_m:
                    for u in range(UNITS):
                        copy_transpose(st, st.m_slot, st.tr_new, u)

            def prologue():
                act.sem_inc(by_t_copied, TR_BANKS)
                for u in range(UNITS):
                    stage_bx(step0, u)
                for u in range(UNITS):
                    copy_transpose(step0, 0, 0, u)

            for_all_steps(act, body, prologue)

        @block.vector
        def _(dve):
            def add_mixed(st, slot, unit0, u):
                dve.wait_ge(mixed, st.count(2 * UNITS, unit0 + u + 1))
                dst = pixel_unit(slot, u)
                src = mix_psum[u % MIX_BANKS][:, :].rearrange("s (g q) -> s q g", g=AG)
                nc.vector.tensor_tensor(dst, src, dst, ALU.add).then_inc(added, 1)

            def bx_in_pixels(st):
                for j in range(STAGE):
                    dve.wait_ge(bx_moved[j], st.count(2 * BG * DMA, 2 * BG * DMA))

            def body(st):
                e = st.e_slot
                dve.wait_ge(kscal_in[st.parity], st.pairs(2 * DMA, DMA * {1: 1, 2: 1, 3: 2, 4: 2}[st.k]))
                dve.wait_ge(added, st.count(2 * UNITS, -UNITS))
                for i in range(RANK):
                    nc.vector.tensor_scalar(out=hk_of(st, i), in0=channel(e, 0), scalar1=k1(st, i, 0), scalar2=None,
                                            op0=ALU.mult).then_inc(hk_added, 1)
                for c in range(1, C):
                    for i in range(RANK):
                        dve.wait_ge(hk_added, st.count(HK_OPS, RANK * (c - 1) + i + 1 - HK_OPS))
                        nc.vector.scalar_tensor_tensor(out=hk_of(st, i), in0=channel(e, c), scalar=k1(st, i, c),
                                                       in1=hk_of(st, i), op0=ALU.mult, op1=ALU.add
                                                       ).then_inc(hk_added, 1)
                dve.wait_ge(hk_added, st.count(HK_OPS))

                def add_term(c, i):
                    return nc.vector.scalar_tensor_tensor(out=channel(e, c), in0=hk_of(st, i), scalar=k2(st, i, c),
                                                          in1=channel(e, c), op0=ALU.mult, op1=ALU.add)

                dve.wait_ge(scaled, st.count(EARLY_C, FILL_C - EARLY_C))
                for c in range(FILL_C):
                    add_term(c, 0).then_inc(k2_added, 1)
                dve.wait_ge(scaled, st.count(EARLY_C))
                dve.wait_ge(late_scaled, st.count(C - EARLY_C))
                dve.wait_ge(k2_added, st.count(K2_OPS, FILL_C - K2_OPS))
                for u in range(UNITS):
                    add_mixed(st, e, -UNITS, u)
                dve.wait_ge(added, st.count(2 * UNITS))
                units = list(range(UNITS)) if st.has_m else []

                def add_mixed_some(count):
                    if units and len(units) == UNITS:
                        bx_in_pixels(st)
                    for _ in range(min(count, len(units))):
                        add_mixed(st, st.m_slot, 0, units.pop(0))

                for c in range(FILL_C, C):
                    add_term(c, 0).then_inc(k2_added, 1)
                    since = c - ADD_FROM[st.k]
                    if since >= 0 and since % ADD_EVERY == 0:
                        add_mixed_some(1)
                for c in range(POOL_C, C - 1):
                    dve.wait_ge(k2_added, st.count(K2_OPS, c + 1 - K2_OPS))
                    add_term(c, 1).then_inc(k2_added, 1)
                add_mixed_some(1 if st.e_layer == 1 else UNITS)
                dve.wait_ge(k2_added, st.count(K2_OPS))
                dve.wait_ge(v_added, st.count(POOL_C, V_SLOTS))
                add_term(C - 1, 1).then_inc(e_complete, 1)
                add_mixed_some(UNITS)

            def prologue():
                bx_in_pixels(step0)
                for u in range(UNITS):
                    add_mixed(step0, 0, 0, u)

            for_all_steps(dve, body, prologue)

        @block.gpsimd
        def _(pool):
            def build_compact(second, coef, eye, w, step, before):
                grid = compact[:, :].rearrange("p (g c) -> p g c", c=C)
                diag = diag_terms[:, :].rearrange("p (g c) -> p g c", c=C)
                terms = rank_terms[:, :].rearrange("p (g i c) -> p g i c", i=RANK, c=C)
                nc.gpsimd.tensor_tensor(
                    rank_terms[:, :].rearrange("p (g c) -> p g c", c=C),
                    second[:, :].rearrange("p (g c) -> p g c", c=C),
                    coef[:, 0:HALF * RANK].unsqueeze(2).to_broadcast([P, HALF * RANK, C]), ALU.mult).then_inc(step, 1)
                pool.wait_ge(step, before + 1)
                nc.gpsimd.tensor_tensor(grid, terms[:, :, 0, :], terms[:, :, 1, :], ALU.add).then_inc(step, 1)
                nc.gpsimd.tensor_tensor(
                    diag, eye.unsqueeze(1).to_broadcast([P, HALF, C]),
                    coef[:, HALF * RANK:].unsqueeze(2).to_broadcast([P, HALF, C]), ALU.mult).then_inc(step, 1)
                pool.wait_ge(step, before + 3)
                nc.gpsimd.tensor_tensor(grid, grid, diag, ALU.add).then_inc(step, 1)
                pool.wait_ge(step, before + 4)
                if w is not None:
                    nc.gpsimd.tensor_tensor(grid, grid, w.unsqueeze(1).to_broadcast([P, HALF, C]),
                                            ALU.add).then_inc(step, 1)
                    pool.wait_ge(step, before + 5)
                return grid

            def build_b_table(parity, before):
                grid = build_compact(b_second[parity], b_coef[parity], eye_s, None, b_table_step, before)
                nc.gpsimd.tensor_tensor(
                    b_table[parity][:, :].rearrange("p (g s c) -> p g s c", s=G8, c=C),
                    grid.unsqueeze(2).to_broadcast([P, HALF, G8, C]),
                    same_s.unsqueeze(1).unsqueeze(3).to_broadcast([P, HALF, G8, C]), ALU.mult).then_inc(b_built, 1)

            def build_a_half(layer, half, before):
                build_compact(a_second[half], a_coef[half], eye_t, w_eye[:, layer * C:(layer + 1) * C],
                              a_table_step, before)
                nc.gpsimd.tensor_tensor(
                    a_table[layer][:, half * HALF * P:(half + 1) * HALF * P].rearrange("p (g t) -> p g t", t=G8),
                    compact[:, :].unsqueeze(2).to_broadcast([P, HALF * C, G8]),
                    same_t.unsqueeze(1).to_broadcast([P, HALF * C, G8]), ALU.mult).then_inc(a_built, 1)

            def build_b(st):
                par = 1 - st.parity
                loads = {0: 1, 1: 2, 2: 2, 3: 3, 4: 3}[st.k]
                pool.wait_ge(b_raw_in[par], st.pairs(2 * 2 * DMA, loads * 2 * DMA))
                pool.wait_ge(b_built, st.count(1, 1))
                if st.first:
                    pool.wait_ge(a_built, 2)
                else:
                    halves = A_UNITS
                    if st.chunk_start:
                        halves = START_BUILDS.get(st.k, [A_UNITS])[0]
                    elif st.chunk_end and st.k > min(END_BUILDS):
                        halves = A_UNITS + END_BUILDS[st.k][0]
                    pool.wait_ge(a_built, st.ch * A_UNITS + halves)
                    pool.wait_ge(bx_ready, st.count(UNITS))
                build_b_table(par, st.count(B_STEPS, B_STEPS))

            def load_a_raw(ch, layer, half):
                j = (ch * L + layer) * 2 + half
                src = q_second[bass.ds(j, 1)].to_broadcast([C, G8, RAW])
                nc.gpsimd.dma_start(a_second[half][:, :], src).then_inc(a_raw_in[half], DMA)
                nc.gpsimd.dma_start(a_coef[half][:, :], q_coef[bass.ds(j, 1)].rearrange("a p f -> (a p) f")
                                    ).then_inc(a_raw_in[half], DMA)

            def build_a(ch, units, b_tables, free=None):
                start = isinstance(ch, int) and ch == 0
                for j in units:
                    if not (start and j < 2):
                        pool.wait_ge(a_built, ch * A_UNITS + (j - 1))
                        load_a_raw(ch, j // 2, j % 2)
                pool.wait_ge(b_built, b_tables)
                if free is not None:
                    pool.wait_ge(*free)
                for j in units:
                    pool.wait_ge(a_raw_in[j % 2], ch * (L * 2 * DMA) + (j // 2 + 1) * 2 * DMA)
                    if not (start and j == 0):
                        pool.wait_ge(a_built, ch * A_UNITS + j)
                    build_a_half(j // 2, j % 2, ch * (A_UNITS * A_STEPS) + j * A_STEPS)

            def add_v(st):
                pool.wait_ge(added, st.count(2 * UNITS))
                for c in range(POOL_C):
                    pool.wait_ge(v_ready, st.count(POOL_C, c + 1 - POOL_C))
                    pool.wait_ge(k2_added, st.count(K2_OPS, c + 1 - K2_OPS))
                    ch = channel(st.e_slot, c)
                    j = c % V_SLOTS
                    term = nc.gpsimd.tensor_tensor(ch, ch, v[:, j * TC:(j + 1) * TC], ALU.add)
                    term.then_inc(v_added, 1)

            def body(st):
                if not st.pool_late:
                    pool.wait_ge(kscal_in[st.parity], st.pairs(2 * DMA, DMA * {1: 1, 2: 1, 3: 2, 4: 2}[st.k]))
                    pool.wait_ge(transposed, st.transposed())
                    for c in range(EARLY_C, C):
                        pool.wait_ge(hk_added, st.count(HK_OPS, RANK * (c + 1) - HK_OPS))
                        ch = channel(st.e_slot, c)
                        nc.gpsimd.tensor_tensor(ch, ch, kdd(st, c).to_broadcast([P, TC]), ALU.mult
                                                ).then_inc(late_scaled, 1)
                add_v(st)
                if not (st.last and st.k >= 3):
                    build_b(st)
                replaced = (mixed, st.count(2 * UNITS, -UNITS))
                if st.chunk_end and st.k in END_BUILDS:
                    build_a(st.ch + 1, END_BUILDS[st.k], st.count(1, 2), replaced)
                if st.chunk_start and st.k in START_BUILDS:
                    build_a(st.ch, START_BUILDS[st.k], st.count(1, 2), replaced)

            def prologue():
                pool.sem_inc(v_added, V_SLOTS)
                for half in range(2):
                    load_a_raw(0, 0, half)
                pool.wait_ge(consts_in, 2 * DMA)
                w_rows = w_eye[:, :].rearrange("p (l c) -> p l c", c=C)
                nc.gpsimd.tensor_tensor(w_rows, w_rows, eye_t.unsqueeze(1).to_broadcast([P, L, C]),
                                        ALU.add).then_inc(w_eye_ready, 1)
                pool.wait_ge(b_raw_in[0], 2 * DMA)
                build_b_table(0, 0)
                pool.wait_ge(w_eye_ready, 1)
                build_a(0, [0, 1], 1)
                build_b(step0)
                build_a(0, [2, 3], 2)
                build_a(0, [4], 2)

            for_all_steps(pool, body, prologue)


MATMUL_LAYERS, ELEMENT_LAYERS = (0, 2), (1, 3)


def kernel(**inputs):
    import numpy as np
    import concourse.bacc as bacc
    from concourse.bass_utils import run_bass_kernel_spmd

    def per_layer(name):
        return [np.asarray(inputs[f"L{l}_conv_{name}"]) for l in range(L)]

    stiles, halves = S // SC, TG // HALF
    x = np.asarray(inputs["x"]).reshape(C, T, S)
    x_t = x.reshape(C, CHUNKS, G8, TG, stiles, SC).transpose(1, 4, 0, 2, 3, 5).reshape(-1, P, FREE)
    x_s = x.reshape(C, CHUNKS, TC, stiles, SG, G8).transpose(1, 3, 5, 0, 4, 2).reshape(-1, P, FREE)

    q1 = np.stack([a.reshape(CHUNKS, G8, halves, HALF, RANK, C) for a in per_layer("qw1")], 1)
    q2 = np.stack([a.reshape(CHUNKS, G8, halves, HALF, RANK, C) for a in per_layer("qw2")], 1)
    qd = np.stack([a.reshape(CHUNKS, G8, halves, HALF, C) for a in per_layer("qdd")], 1)
    q_second = q2.transpose(0, 1, 3, 2, 4, 5, 6).reshape(-1, G8, RAW)
    q_coef = np.concatenate([q1.transpose(0, 1, 3, 6, 2, 4, 5).reshape(-1, P, HALF * RANK),
                             qd.transpose(0, 1, 3, 5, 2, 4).reshape(-1, P, HALF)], 2)

    k1, k2, kd = per_layer("kw1"), per_layer("kw2"), per_layer("kdd")
    m1 = np.stack([k1[l].reshape(stiles, SG, G8, RANK, C) for l in MATMUL_LAYERS], 1)
    m2 = np.stack([k2[l].reshape(stiles, SG, G8, RANK, C) for l in MATMUL_LAYERS], 1)
    md = np.stack([kd[l].reshape(stiles, SG, G8, C) for l in MATMUL_LAYERS], 1)
    k_second = m2.transpose(0, 1, 3, 2, 4, 5).reshape(-1, G8, RAW)
    k_coef = np.concatenate([m1.transpose(0, 1, 3, 5, 2, 4).reshape(-1, P, SG * RANK),
                             md.transpose(0, 1, 3, 4, 2).reshape(-1, P, SG)], 2)
    k_scalars = np.stack([np.concatenate([k1[l].reshape(stiles, SC, RANK * C), k2[l].reshape(stiles, SC, RANK * C),
                                          kd[l].reshape(stiles, SC, C)], 2) for l in ELEMENT_LAYERS], 1)
    k_scalars = k_scalars.reshape(-1, P, KS)
    w = np.stack([a.reshape(C, C) for a in per_layer("w")], 1).reshape(C, L * C)

    p = np.arange(P)[:, None]
    shapes = np.concatenate([p == np.arange(P), p % G8 == np.arange(G8), p // C == np.arange(G8),
                             p // G8 == np.arange(C), p % C == np.arange(C)], 1).astype(np.float32)

    nc = bacc.Bacc("TRN2", target_bir_lowering=False, num_devices=1)
    arrays, args = {}, []
    for name, a in (("x_t", x_t), ("x_s", x_s), ("q_second", q_second), ("q_coef", q_coef), ("k_second", k_second),
                    ("k_coef", k_coef), ("k_scalars", k_scalars), ("w", w), ("shapes", shapes)):
        arrays[name] = np.ascontiguousarray(a)
        args.append(nc.dram_tensor(name, a.shape, F32, kind="ExternalInput").ap())
    args.append(nc.dram_tensor("out", (CHUNKS * stiles, P, FREE), F32, kind="ExternalOutput").ap())
    build_program(nc, *args)
    result = run_bass_kernel_spmd(nc, [arrays], core_ids=[0]).results[0]["out"]
    return result.reshape(CHUNKS, stiles, SC, C, TC).transpose(3, 0, 4, 1, 2).reshape(1, C, T, S)
```
